# Optimizing a Trainium2 kernel written in Bass

```python
import numpy as np
import jax
import jax.numpy as jnp

def _softmax(x, axis=-1):
    return jax.nn.softmax(x, axis=axis)

def _gelu(x):
    return jax.nn.gelu(x, approximate=True)

def _silu(x):
    return jax.nn.silu(x)

def _sigmoid(x):
    return jax.nn.sigmoid(x)

def _layernorm(x, axis=-1, eps=1e-05):
    m = jnp.mean(x, axis=axis, keepdims=True)
    v = jnp.var(x, axis=axis, keepdims=True)
    return (x - m) / jnp.sqrt(v + eps)

def _scatter_add(tgt, idx, src, axis=0):
    return tgt.at[idx].add(src)

def _segment_sum(src, seg, n):
    return jax.ops.segment_sum(src, seg, n)
kernel_name = 'mk_seq_postln_d1_jaxref_r4_28171b'

def setup_inputs(seed: int=0):
    np.random.seed(seed)
    _w = jnp.asarray

    def _L0_attn_setup():
        import jax, jax.numpy as jnp
        import numpy as np
        ETA = 0.01
        ALPHA = 0.95
        THRESHOLD = 1.0
        B, S, IN, OUT = (4, 512, 512, 512)

        def _reference_tuple_inner(x, W, target_W, delta_W):
            y = jnp.einsum('bsi,oi->bso', x, W + delta_W)
            predicted = jnp.einsum('bsi,oi->bso', x, target_W)
            teach = y - predicted
            surprise = jnp.mean(jnp.linalg.norm(teach, axis=-1))
            denom = jnp.float32(B * S)
            delta = jnp.einsum('bso,bsi->oi', teach, x) / denom
            new_delta_W = jnp.where(surprise > THRESHOLD, ALPHA * delta_W + ETA * delta, delta_W)
            return (y, new_delta_W)
        key = jax.random.key(seed)
        k1, k2, k3, k4 = jax.random.split(key, 4)
        bound = 1.0 / np.sqrt(IN)
        x = jax.random.normal(k1, (B, S, IN), dtype=jnp.float32)
        W = jax.random.uniform(k2, (OUT, IN), jnp.float32, -bound, bound)
        target_W = jax.random.uniform(k3, (OUT, IN), jnp.float32, -bound, bound)
        delta_W = 0.01 * jax.random.normal(k4, (OUT, IN), dtype=jnp.float32)
        return {'x': x, 'W': W, 'target_W': target_W, 'delta_W': delta_W}
    _L0_attn_in = _L0_attn_setup()

    def _L0_ffn_setup():
        import jax, jax.numpy as jnp
        import numpy as np
        TARGET_SPARSITY = 0.9
        LN_EPS = 1e-05

        def ternary_quant(W):
            scale = jnp.mean(jnp.abs(W))
            q = jnp.clip(jnp.round(W / (scale + 1e-08)), -1.0, 1.0) * scale
            return W + jax.lax.stop_gradient(q - W)

        def layernorm(x, gamma, beta):
            mu = jnp.mean(x, axis=-1, keepdims=True)
            var = jnp.var(x, axis=-1, keepdims=True)
            return (x - mu) * jax.lax.rsqrt(var + LN_EPS) * gamma + beta
        key = jax.random.key(seed)
        ks = jax.random.split(key, 3)
        B, S, D, N = (4, 512, 512, 2048)
        x = jax.random.normal(ks[0], (B, S, D), dtype=jnp.float32)
        W_syn = jax.random.normal(ks[1], (N, D), dtype=jnp.float32) * (1.0 / np.sqrt(D))
        b_syn = jnp.zeros((N,), dtype=jnp.float32)
        W_out = jax.random.normal(ks[2], (D, N), dtype=jnp.float32) * (1.0 / np.sqrt(N))
        b_out = jnp.zeros((D,), dtype=jnp.float32)
        gamma = jnp.ones((D,), dtype=jnp.float32)
        beta = jnp.zeros((D,), dtype=jnp.float32)
        return {'x': x, 'W_syn': W_syn, 'b_syn': b_syn, 'W_out': W_out, 'b_out': b_out, 'gamma': gamma, 'beta': beta}
    _L0_ffn_in = _L0_ffn_setup()
    _d = {'L0_attn_x': _L0_attn_in['x'], 'L0_attn_W': _L0_attn_in['W'], 'L0_attn_target_W': _L0_attn_in['target_W'], 'L0_attn_delta_W': _L0_attn_in['delta_W'], 'L0_ffn_W_syn': _L0_ffn_in['W_syn'], 'L0_ffn_b_syn': _L0_ffn_in['b_syn'], 'L0_ffn_W_out': _L0_ffn_in['W_out'], 'L0_ffn_b_out': _L0_ffn_in['b_out'], 'L0_ffn_gamma': _L0_ffn_in['gamma'], 'L0_ffn_beta': _L0_ffn_in['beta']}
    _x0 = _d['L0_attn_x']
    _d['L0_attn_x'] = jax.random.normal(jax.random.fold_in(jax.random.key(seed), 1), (8, 512, 512), dtype=_x0.dtype)
    del _x0
    return _d

def reference(L0_attn_x, L0_attn_W, L0_attn_target_W, L0_attn_delta_W, L0_ffn_W_syn, L0_ffn_b_syn, L0_ffn_W_out, L0_ffn_b_out, L0_ffn_gamma, L0_ffn_beta):

    def _L0_attn_ref(x, W, target_W, delta_W):
        import jax, jax.numpy as jnp
        import numpy as np
        ETA = 0.01
        ALPHA = 0.95
        THRESHOLD = 1.0
        B, S, IN, OUT = (4, 512, 512, 512)

        def _reference_tuple_inner(x, W, target_W, delta_W):
            y = jnp.einsum('bsi,oi->bso', x, W + delta_W)
            predicted = jnp.einsum('bsi,oi->bso', x, target_W)
            teach = y - predicted
            surprise = jnp.mean(jnp.linalg.norm(teach, axis=-1))
            denom = jnp.float32(B * S)
            delta = jnp.einsum('bso,bsi->oi', teach, x) / denom
            new_delta_W = jnp.where(surprise > THRESHOLD, ALPHA * delta_W + ETA * delta, delta_W)
            return (y, new_delta_W)
        return _reference_tuple_inner(x, W, target_W, delta_W)[0]

    def _L0_ffn_ref(x, W_syn, b_syn, W_out, b_out, gamma, beta):
        import jax, jax.numpy as jnp
        import numpy as np
        TARGET_SPARSITY = 0.9
        LN_EPS = 1e-05

        def ternary_quant(W):
            scale = jnp.mean(jnp.abs(W))
            q = jnp.clip(jnp.round(W / (scale + 1e-08)), -1.0, 1.0) * scale
            return W + jax.lax.stop_gradient(q - W)

        def layernorm(x, gamma, beta):
            mu = jnp.mean(x, axis=-1, keepdims=True)
            var = jnp.var(x, axis=-1, keepdims=True)
            return (x - mu) * jax.lax.rsqrt(var + LN_EPS) * gamma + beta
        B, S, D = x.shape
        N = W_syn.shape[0]
        x_flat = x.reshape(-1, D)
        z = x_flat @ ternary_quant(W_syn).T + b_syn
        k = max(1, int(N * (1.0 - TARGET_SPARSITY)))
        topv, _ = jax.lax.top_k(z, k)
        thresh = topv[:, -1:]
        hidden = jnp.where(z >= thresh, jax.nn.relu(z), 0.0)
        out = hidden @ ternary_quant(W_out).T + b_out
        out = out.reshape(B, S, D)
        return layernorm(x + out, gamma, beta)
    x = L0_attn_x
    x = _layernorm(x + _L0_attn_ref(x, L0_attn_W, L0_attn_target_W, L0_attn_delta_W), axis=-1)
    x = _layernorm(x + _L0_ffn_ref(x, L0_ffn_W_syn, L0_ffn_b_syn, L0_ffn_W_out, L0_ffn_b_out, L0_ffn_gamma, L0_ffn_beta), axis=-1)
    return x

_drawn_inputs = setup_inputs


def setup_inputs(seed=0):
    import zlib

    import numpy as np

    out = dict(_drawn_inputs(seed))
    spreads = {'L0_ffn_b_syn': (0.0, 0.1),
     'L0_ffn_b_out': (0.0, 0.1),
     'L0_ffn_gamma': (1.0, 0.2),
     'L0_ffn_beta': (0.0, 0.1)}
    factors = {}
    for name, (base, spread) in spreads.items():
        noise = np.random.default_rng([zlib.crc32(name.encode()), seed]).standard_normal(out[name].shape)
        drawn = base * np.exp(spread * noise) if base else spread * noise
        out[name] = jnp.asarray(drawn.astype(out[name].dtype))
    for name, factor in factors.items():
        out[name] = (out[name] * factor).astype(out[name].dtype)
    return out
```

```python
import concourse.bass as bass
from concourse import mybir
from contextlib import ExitStack

FP32 = mybir.dt.float32
FP16 = mybir.dt.float16
I32 = mybir.dt.int32
ALU = mybir.AluOpType
ACT = mybir.ActivationFunctionType

P = 128
TOK, D, N = 4096, 512, 2048
TILES = TOK // P
PAIRS = TILES // 2
KD = D // P
KN = N // P
QB = 4
NQ = KN // QB
BANK = 512
HALF = N // 2
TOPK = max(1, int(N * (1.0 - 0.9)))
LN_EPS = 1e-5
X_SCALE = 512.0
H_LIMIT = 16384.0

ROUNDS = 5
SPREAD = 1.27
MIDDLE = TOPK - 4.5
SIGN_MID = 2 * MIDDLE - N
SLOPE = 0.9 / (2 * N * 0.1755)
DAMP = 0.4
T_MIN = 1e-18
LOWEST = -3.0e38


def postln_kernel(nc, x, xT, wT, dwT, w_synT, b_syn, w_outT, b_out, gamma, beta, out):
    ctx = ExitStack()
    with ctx:
        def sb(name, shape, dt=FP32):
            return ctx.enter_context(nc.sbuf_tensor(name, shape, dt))

        def pb(name, shape, dt=FP32):
            return ctx.enter_context(nc.psum_tensor(name, shape, dt))

        def sem(name):
            return ctx.enter_context(nc.semaphore(name))

        def sem2(name):
            return [sem(f"{name}{j}") for j in range(2)]

        ZS, XS = 3, 4
        zring = sb("zring", [P, ZS * 2 * N])
        w_sb = sb("w_sb", [P, N])
        h_sb = sb("h_sb", [P, 2 * N])
        junk = sb("junk", [P, 2, N], FP16)
        t_syn = sb("t_syn", [P, KD, N], FP16)
        t_out = sb("t_out", [P, KN, D], FP16)
        weff = sb("weff", [P, KD, D])
        bias_z = sb("bias_z", [P, N])
        bout_bc = sb("bout_bc", [P, D])
        gamma_bc = sb("gamma_bc", [P, D])
        beta_bc = sb("beta_bc", [P, D])
        xT_sb = sb("xT_sb", [P, KD, 2 * P])
        x_sb = sb("x_sb", [P, 2, D])
        u_sb = sb("u_sb", [P, 2, D])
        x1_sb = sb("x1_sb", [P, 2, D])
        x1b = sb("x1b", [P, XS * 2 * D])
        x1g = sb("x1g", [P, XS * 2 * D])
        x1hi = sb("x1hi", [P, 2, KD, P], FP16)
        x1lo = sb("x1lo", [P, 2, KD, P], FP16)
        hhi = sb("hhi", [P, NQ, QB, P], FP16)
        hlo = sb("hlo", [P, NQ, QB, P], FP16)
        r_sb = sb("r_sb", [P, 2, D])
        y_sb = sb("y_sb", [P, 2, D])
        ident = sb("ident", [P, P])
        ones = sb("ones", [P, P])
        place = sb("place", [P, 8])
        cst = sb("cst", [P, 2])
        st1, st2, st3 = (sb(f"st{k}", [P, 2, 6]) for k in (1, 2, 3))
        mv1, mv2, mv3 = (sb(f"mv{k}", [P, 2, 2]) for k in (1, 2, 3))
        rs1, rs2, rs3 = (sb(f"rs{k}", [P, 2, 2]) for k in (1, 2, 3))
        zsum = sb("zsum", [P, 2, 2])
        zsq = sb("zsq", [P, 2])
        tq = sb("tq", [P, 2, 8])
        negt = sb("negt", [P, 2])
        ngh = sb("ngh", [P, 2])
        dev = sb("dev", [P, 2, 2])
        signs = sb("signs", [P, 2])
        signs_fin = sb("signs_fin", [P, 2])
        t_fin = sb("t_fin", [P, 2])
        m8 = sb("m8", [P, 2, 8])
        pick = sb("pick", [P, 2, 8])
        hit = sb("hit", [P, 2])
        ok = sb("ok", [P, 2])
        thr = sb("thr", [P, 2])
        flag = sb("flag", [1, 2], I32)
        psyn = sb("psyn", [P, KD])
        pout = sb("pout", [P, 4])
        part = sb("part", [P, 2])
        sc = sb("sc", [P, 12])

        z_ps = pb("z_ps", [P, 2, HALF])
        tr_ps = [pb(f"tr_ps{k}", [P, BANK]) for k in range(2)]
        u_ps = pb("u_ps", [P, BANK])
        o_ps = pb("o_ps", [P, BANK])

        neg = x1b[:, 3 * 2 * D:3 * 2 * D + N // 2].bitcast(FP16)
        syn_in = [zring[:, k * N:(k + 1) * N] for k in range(KD)]
        out_in = [zring[:, (KD + k) * N:(KD + k + 1) * N] for k in range(2)] + \
                 [h_sb[:, k * N:(k + 1) * N] for k in range(2)]
        dw_in = w_sb[:, 0:KD * D].rearrange("p (k n) -> p k n", k=KD)

        x_loaded = sem("x_loaded")
        weff_loaded = sem("weff_loaded")
        syn_loaded = [sem(f"syn_loaded{k}") for k in range(KD)]
        out_loaded = [sem(f"out_loaded{k}") for k in range(4)]
        vec_loaded = sem("vec_loaded")
        bsyn_loaded = sem("bsyn_loaded")
        stored = sem("stored")
        consts_made = sem("consts_made")
        weff_made = sem("weff_made")
        abs_summed = sem("abs_summed")
        part_summed = sem("part_summed")
        sums_ready = sem("sums_ready")
        t_syn_made = sem("t_syn_made")
        t_out_made = sem("t_out_made")
        setup_step = sem("setup_step")
        pool_setup = sem("pool_setup")
        u_ready = sem("u_ready")
        u_read = sem("u_read")
        u_done = sem("u_done")
        ln1_bn = sem("ln1_bn")
        ln1_stats = sem("ln1_stats")
        ln1_rstd = sem("ln1_rstd")
        x1_ready = sem("x1_ready")
        x1_adds = sem("x1_adds")
        x1T_ready = sem("x1T_ready")
        x_hi = sem("x_hi")
        x_lo = sem("x_lo")
        z_ready = sem("z_ready")
        z_evac = sem("z_evac")
        squared = sem("squared")
        t_ready = sem2("t_ready")
        t_step = sem2("t_step")
        counted = sem2("counted")
        masked = sem("masked")
        max8_done = sem("max8_done")
        picked = sem("picked")
        hit_done = sem("hit_done")
        selected = sem("selected")
        flag_ready = sem("flag_ready")
        flag_read = sem("flag_read")
        fb_step = sem("fb_step")
        h_ready = sem("h_ready")
        hT_ready = sem("hT_ready")
        h_hi = sem("h_hi")
        h_lo = sem("h_lo")
        m3_done = sem("m3_done")
        o_read = sem("o_read")
        ln2_bn = sem("ln2_bn")
        ln2_stats = sem("ln2_stats")
        ln2_rstd = sem("ln2_rstd")
        centred = sem("centred")
        v_done = sem("v_done")
        ln3_bn = sem("ln3_bn")
        ln3_stats = sem("ln3_stats")
        ln3_rstd = sem("ln3_rstd")
        y_ready = sem("y_ready")
        apart = sem("apart")
        eps_step = [sem(f"eps_step{k}") for k in range(3)]

        def wait(eng, s, value):
            if isinstance(value, int) and value <= 0:
                return
            eng.wait_ge(s, value)

        def wait_apart(eng, s, value):
            wait(eng, s, value)
            if not isinstance(value, int):
                eng.sem_inc(apart, 1)

        def zslot(pair, j):
            return (pair % ZS) * (2 * N) + j * N

        def xslot(pair, j):
            return (pair % XS) * (2 * D) + j * D

        def windows(eng, body, ahead=1):
            def stages(i):
                return (0 <= i + ahead < PAIRS, 0 <= i < PAIRS, 0 <= i - 1 < PAIRS, 0 <= i - 2 < PAIRS)
            full = [i for i in range(-1, PAIRS + 2) if all(stages(i))][1:]
            for i in range(-1, full[0]):
                body(i, *stages(i))
            with eng.Fori(full[0], full[-1] + 1) as i:
                body(i, True, True, True, True)
            for i in range(full[-1] + 1, PAIRS + 2):
                body(i, *stages(i))

        block = ctx.enter_context(nc.Block())

        @block.sync
        def _(sp):
            xT_v = xT.rearrange("(k p) t -> p k t", p=P)
            x_v = x.rearrange("(t p) d -> p t d", p=P)
            out_v = out.rearrange("(t p) d -> p t d", p=P)
            syn_v = w_synT.rearrange("(k p) n -> p k n", p=P)
            outw_v = w_outT.rearrange("(k p) d -> p k d", p=P)
            for k in range(KD):
                sp.dma_start(syn_in[k], syn_v[:, k, :]).then_inc(syn_loaded[k], 16)
            sp.dma_start(weff[:, :, :], wT.rearrange("(k p) n -> p k n", p=P)).then_inc(weff_loaded, 16)
            sp.dma_start(dw_in, dwT.rearrange("(k p) n -> p k n", p=P)).then_inc(weff_loaded, 16)

            def load(pair):
                wait_apart(sp, x_loaded, 32 * pair)
                wait_apart(sp, u_ready, 2 * pair)
                wait_apart(sp, u_read, 2 * pair)
                sp.dma_start(xT_sb[:, :, :], xT_v[:, :, bass.ds(pair * (2 * P), 2 * P)]).then_inc(x_loaded, 16)
                sp.dma_start(x_sb[:, :, :], x_v[:, bass.ds(pair * 2, 2), :]).then_inc(x_loaded, 16)

            load(0)
            sp.dma_start(bias_z[:, :], b_syn.rearrange("(a n) -> a n", a=1).broadcast_to([P, N])).then_inc(bsyn_loaded, 16)
            for k in range(4):
                dst = out_in[k].rearrange("p (c d) -> p c d", d=D)
                sp.dma_start(dst, outw_v[:, QB * k:QB * (k + 1), :]).then_inc(out_loaded[k], 16)
            for dst, src in ((bout_bc, b_out), (gamma_bc, gamma), (beta_bc, beta)):
                sp.dma_start(dst[:, :], src.rearrange("(a n) -> a n", a=1).broadcast_to([P, D])).then_inc(vec_loaded, 16)

            def body(i, A, B, S, Dd):
                if A:
                    load(i + 2)
                if Dd:
                    for j in range(2):
                        t = 2 * (i - 2) + j
                        wait_apart(sp, y_ready, t + 1)
                        wait_apart(sp, stored, 16 * t)
                        sp.dma_start(out_v[:, t, :] if isinstance(t, int) else out_v[:, bass.ds(t, 1), :],
                                     y_sb[:, j, :] if isinstance(t, int) else y_sb[:, j:j + 1, :]).then_inc(stored, 16)

            windows(sp, body, ahead=2)
            sp.wait_ge(stored, 16 * TILES)

        @block.gpsimd
        def _(pool):
            g = nc.gpsimd
            g.memset(ident[:, :], 0.0).then_inc(pool_setup, 1)
            g.memset(ones[:, :], 1.0).then_inc(pool_setup, 1)
            g.memset(cst[:, 0:1], -0.5).then_inc(pool_setup, 1)
            g.memset(cst[:, 1:2], 0.5).then_inc(pool_setup, 1)
            for k in range(8):
                g.memset(place[:, k:k + 1], float(2 * (TOPK - 1 - k) - N)).then_inc(pool_setup, 1)
            pool.wait_ge(pool_setup, 12)
            g.affine_select(out=ident[:, :], in_=ident[:, :], compare_op=ALU.not_equal, fill=1.0, base=0,
                            pattern=[[-1, P]], channel_multiplier=1).then_inc(consts_made, 1)
            pool.wait_ge(consts_made, 1)

            def rstd(k, t, j, stats, mv, rs, done):
                wait_apart(pool, stats, t + 1)
                g.tensor_scalar(rs[:, j, 1:2], mv[:, j, 1:2], LN_EPS, None, ALU.add).then_inc(eps_step[k], 1)
                pool.wait_ge(eps_step[k], t + 1)
                g.tensor_tensor(rs[:, j, 0:1], rs[:, j, 1:2], cst[:, 0:1], ALU.pow).then_inc(done, 1)

            def first(pair, j):
                t = 2 * pair + j
                q = lambda c: tq[:, j, c:c + 1]
                wait_apart(pool, squared, t + 1)
                link(j, pair, g.tensor_tensor(q(0), zsum[:, j, 0:1], zsum[:, j, 1:2], ALU.add))
                link(j, pair, g.tensor_scalar(q(1), q(0), 1.0 / N, None, ALU.mult))
                link(j, pair, g.tensor_tensor(q(2), q(1), q(1), ALU.mult))
                link(j, pair, g.tensor_scalar(q(3), zsq[:, j:j + 1], 1.0 / N, q(2), ALU.mult, ALU.subtract))
                link(j, pair, g.tensor_scalar(q(4), q(3), 0.0, None, ALU.max))
                link(j, pair, g.tensor_tensor(q(5), q(4), cst[:, 1:2], ALU.pow))
                link(j, pair, g.tensor_scalar(q(6), q(5), SPREAD, q(1), ALU.mult, ALU.add))
                link(j, pair, g.tensor_scalar(ngh[:, j:j + 1], q(5), -SLOPE, None, ALU.mult))
                link(j, pair, g.tensor_scalar(dev[:, j, 0:1], q(5), 0.0, None, ALU.mult))
                g.tensor_scalar(negt[:, j:j + 1], q(6), -1.0, -T_MIN, ALU.mult, ALU.min).then_inc(t_ready[j], 1)

            def update(pair, j, r):
                q = lambda c: tq[:, j, c:c + 1]
                new, old = dev[:, j, r % 2:r % 2 + 1], dev[:, j, (r + 1) % 2:(r + 1) % 2 + 1]
                wait_apart(pool, counted[j], ROUNDS * pair + r)
                link(j, pair, g.tensor_scalar(new, signs[:, j:j + 1], -SIGN_MID, None, ALU.add))
                if r > 1:
                    link(j, pair, g.tensor_tensor(q(0), new, old, ALU.mult))
                    link(j, pair, g.tensor_scalar(q(1), q(0), 0.0, -DAMP, ALU.is_lt, ALU.mult))
                    link(j, pair, g.tensor_scalar(ngh[:, j:j + 1], q(1), 1.0, ngh[:, j:j + 1], ALU.add, ALU.mult))
                link(j, pair, g.tensor_tensor(q(2), new, new, ALU.mult))
                link(j, pair, g.tensor_scalar(q(3), q(2), 8.5 ** 2, ngh[:, j:j + 1], ALU.is_gt, ALU.mult))
                link(j, pair, g.tensor_scalar(q(4), new, q(3), negt[:, j:j + 1], ALU.mult, ALU.add))
                if r < ROUNDS - 1:
                    g.tensor_scalar(negt[:, j:j + 1], q(4), -T_MIN, None, ALU.min).then_inc(t_ready[j], 1)
                else:
                    link(j, pair, g.tensor_scalar(negt[:, j:j + 1], q(4), -T_MIN, None, ALU.min))
                    wait_apart(pool, selected, 2 * pair + j - 1)
                    g.tensor_scalar(t_fin[:, j:j + 1], negt[:, j:j + 1], -1.0, None, ALU.mult).then_inc(t_ready[j], 1)

            LINKS = 9 + 4 + 7 * (ROUNDS - 2) + 1
            nth = [0, 0]

            def link(j, pair, ins):
                nth[j] += 1
                ins.then_inc(t_step[j], 1)
                wait_apart(pool, t_step[j], LINKS * pair + nth[j])

            def adds(i, j):
                t = 2 * (i + 1) + j
                wait_apart(pool, x1_ready, t + 1)
                if isinstance(i, int) and i == -1 and j == 0:
                    pool.wait_ge(vec_loaded, 48)
                g.tensor_tensor(x1b[:, bass.ds(xslot(i + 1, j), D)], x1_sb[:, j, :], bout_bc[:, :], ALU.add)
                g.tensor_tensor(x1g[:, bass.ds(xslot(i + 1, j), D)], x1_sb[:, j, :], beta_bc[:, :], ALU.add)\
                    .then_inc(x1_adds, 1)

            def body(i, A, B, S, Dd):
                nth[0] = nth[1] = 0
                a, d = 2 * (i + 1), 2 * (i - 2)
                if B:
                    first(i, 0)
                    first(i, 1)
                if A:
                    rstd(0, a, 0, ln1_stats, mv1, rs1, ln1_rstd)
                if B:
                    update(i, 0, 1)
                    update(i, 1, 1)
                if A:
                    rstd(0, a + 1, 1, ln1_stats, mv1, rs1, ln1_rstd)
                    adds(i, 0)
                if B:
                    update(i, 0, 2)
                if A:
                    adds(i, 1)
                if B:
                    update(i, 1, 2)
                if Dd:
                    rstd(1, d, 0, ln2_stats, mv2, rs2, ln2_rstd)
                if B:
                    update(i, 0, 3)
                    update(i, 1, 3)
                if Dd:
                    rstd(2, d, 0, ln3_stats, mv3, rs3, ln3_rstd)
                if B:
                    update(i, 0, 4)
                    update(i, 1, 4)
                if Dd:
                    rstd(1, d + 1, 1, ln2_stats, mv2, rs2, ln2_rstd)
                    rstd(2, d + 1, 1, ln3_stats, mv3, rs3, ln3_rstd)

            windows(pool, body)

        @block.scalar
        def _(act):
            for k in range(KD):
                act.wait_ge(syn_loaded[k], 16)
                wait(act, abs_summed, k - 1)
                nc.scalar.activation(junk[:, k % 2, :], syn_in[k], ACT.Abs, accum_out=psyn[:, k:k + 1]).then_inc(abs_summed, 1)

            def square(pair, j):
                t = 2 * pair + j
                wait_apart(act, z_evac, 2 * t + 2)
                if isinstance(pair, int) and pair == 0:
                    act.wait_ge(abs_summed, KD + 4)
                wait_apart(act, counted[j], ROUNDS * pair)
                nc.scalar.activation(junk[:, j, :], zring[:, bass.ds(zslot(pair, j), N)], ACT.Square,
                                     accum_out=zsq[:, j:j + 1]).then_inc(squared, 1)

            def count(pair, j, r):
                wait_apart(act, t_ready[j], ROUNDS * pair + r + 1)
                dst = signs if r < ROUNDS - 1 else signs_fin
                nc.scalar.activation(junk[:, j, :], zring[:, bass.ds(zslot(pair, j), N)], ACT.Sign,
                                     bias=negt[:, j:j + 1], accum_out=dst[:, j:j + 1]).then_inc(counted[j], 1)

            def hi_x(t, j):
                wait(act, x1T_ready, t + 1)
                wait(act, z_ready, 2 * t - 2)
                nc.scalar.activation(x1hi[:, j, :, :], tr_ps[0][:, :].rearrange("p (k t) -> p k t", k=KD), ACT.Copy,
                                     scale=X_SCALE).then_inc(x_hi, 1)

            def hi_h(t, q):
                wait(act, hT_ready, 4 * t + q + 1)
                wait(act, m3_done, 4 * t + q - 3)
                nc.scalar.activation(hhi[:, q, :, :], tr_ps[q % 2][:, :].rearrange("p (k t) -> p k t", k=QB),
                                     ACT.Copy).then_inc(h_hi, 1)

            def body(i, A, B, S, Dd):
                def c(j, r):
                    if B:
                        count(i, j, r)

                if B:
                    square(i, 0)
                    square(i, 1)
                c(0, 0)
                c(1, 0)
                c(0, 1)
                for j, between in ((0, ((1, 1), (0, 2), (1, 2))), (1, ((0, 4), (1, 4), None))):
                    a, d = 2 * (i + 1) + j, 2 * (i - 2) + j
                    if Dd:
                        hi_h(d, 0)
                        hi_h(d, 1)
                    if between[0]:
                        c(*between[0])
                    if Dd:
                        hi_h(d, 2)
                    if between[1]:
                        c(*between[1])
                    if Dd:
                        hi_h(d, 3)
                    if A:
                        hi_x(a, j)
                    if between[2]:
                        c(*between[2])
                    if j == 0:
                        c(0, 3)
                        c(1, 3)
                if isinstance(i, int) and i == -1:
                    for k in range(4):
                        act.wait_ge(out_loaded[k], 16)
                        act.wait_ge(abs_summed, KD + k - 1)
                        nc.scalar.activation(junk[:, k % 2, :], out_in[k], ACT.Abs, accum_out=pout[:, k:k + 1])\
                            .then_inc(abs_summed, 1)

            windows(act, body)

        @block.vector
        def _(dve):
            v = nc.vector
            nstep = [0]

            def link(ins):
                nstep[0] += 1
                ins.then_inc(setup_step, 1)
                dve.wait_ge(setup_step, nstep[0])

            dve.wait_ge(weff_loaded, 32)
            v.tensor_tensor(weff[:, :, :], weff[:, :, :], dw_in, ALU.add).then_inc(weff_made, 1)
            dve.wait_ge(abs_summed, KD)
            v.tensor_reduce(part[:, 0:1], psyn[:, :], mybir.AxisListType.X, ALU.add).then_inc(part_summed, 1)
            dve.wait_ge(sums_ready, 1)
            link(v.tensor_scalar(sc[:, 0:1], u_ps[:, 0:1], 1.0 / (N * D), None, ALU.mult))
            link(v.tensor_scalar(sc[:, 1:2], sc[:, 0:1], 1e-8, 0.5, ALU.add, ALU.mult))
            link(v.tensor_scalar(sc[:, 2:3], sc[:, 1:2], -1.0, None, ALU.mult))

            def ternary(dst, src, hi, lo, done, k):
                wait(dve, done, k)
                link(v.tensor_scalar(neg[:, :], src, lo, None, ALU.is_lt))
                v.scalar_tensor_tensor(dst, src, hi, neg[:, :], ALU.is_gt, ALU.subtract).then_inc(done, 1)

            for k in range(KD):
                ternary(t_syn[:, k, :], syn_in[k], sc[:, 1:2], sc[:, 2:3], t_syn_made, k)
            dve.wait_ge(bsyn_loaded, 16)
            link(v.tensor_reduce(sc[:, 3:4], bias_z[:, :], mybir.AxisListType.X, ALU.max))
            link(v.tensor_scalar(sc[:, 3:4], sc[:, 3:4], 0.0, None, ALU.max))
            link(v.scalar_tensor_tensor(sc[:, 4:5], sc[:, 0:1], float(D), sc[:, 3:4], ALU.mult, ALU.add))
            link(v.tensor_scalar(sc[:, 4:5], sc[:, 4:5], 1e-20, None, ALU.max))
            link(v.tensor_scalar(sc[:, 5:6].bitcast(I32), sc[:, 4:5].bitcast(I32), 0x7F800000, None, ALU.bitwise_and))
            link(v.reciprocal(sc[:, 6:7], sc[:, 5:6]))
            link(v.tensor_scalar(sc[:, 6:7], sc[:, 6:7], H_LIMIT, None, ALU.mult))
            link(v.tensor_scalar(bias_z[:, :], bias_z[:, :], sc[:, 6:7], None, ALU.mult))
            link(v.tensor_scalar(sc[:, 7:8], sc[:, 0:1], sc[:, 6:7], 1.0 / X_SCALE, ALU.mult, ALU.mult))

            def out_weights():
                dve.wait_ge(abs_summed, KD + 4)
                v.tensor_reduce(part[:, 1:2], pout[:, :], mybir.AxisListType.X, ALU.add).then_inc(part_summed, 1)
                dve.wait_ge(sums_ready, 2)
                link(v.tensor_scalar(sc[:, 8:9], o_ps[:, 0:1], 1.0 / (N * D), None, ALU.mult))
                link(v.tensor_scalar(sc[:, 9:10], sc[:, 8:9], 1e-8, 0.5, ALU.add, ALU.mult))
                link(v.tensor_scalar(sc[:, 10:11], sc[:, 9:10], -1.0, None, ALU.mult))
                link(v.tensor_scalar(sc[:, 11:12], sc[:, 5:6], sc[:, 8:9], 1.0 / H_LIMIT, ALU.mult, ALU.mult))
                for k in range(4):
                    ternary(t_out[:, QB * k:QB * (k + 1), :].rearrange("p c d -> p (c d)"), out_in[k],
                            sc[:, 9:10], sc[:, 10:11], t_out_made, k)

            def bn(st, mv, src, step, done, t, j):
                v.bn_stats(st[:, j, :], src).then_inc(step, 1)
                wait_apart(dve, step, t + 1)
                v.bn_aggr(mv[:, j, :], st[:, j, :]).then_inc(done, 1)

            def ln1_in(i, j):
                t = 2 * (i + 1) + j
                dve.wait_ge(x_loaded, 32 * (i + 2))
                dve.wait_ge(u_ready, t + 1)
                v.tensor_tensor(u_sb[:, j, :], u_ps[:, :], x_sb[:, j, :], ALU.add).then_inc(u_read, 1)
                dve.wait_ge(u_read, t + 1)
                bn(st1, mv1, u_sb[:, j, :], ln1_bn, ln1_stats, t, j)

            def ln1_out(i, j):
                t = 2 * (i + 1) + j
                dve.wait_ge(ln1_rstd, t + 1)
                wait(dve, x1T_ready, t - 1)
                wait(dve, x1_adds, t - 1)
                v.tensor_scalar(x1_sb[:, j, :], u_sb[:, j, :], mv1[:, j, 0:1], rs1[:, j, 0:1],
                                ALU.subtract, ALU.mult).then_inc(x1_ready, 1)

            def lo_x(i, j):
                t = 2 * (i + 1) + j
                dve.wait_ge(x_hi, t + 1)
                wait(dve, z_ready, 2 * t - 2)
                v.scalar_tensor_tensor(x1lo[:, j, :, :].rearrange("p k t -> p (k t)"), tr_ps[0][:, :], X_SCALE,
                                       x1hi[:, j, :, :].rearrange("p k t -> p (k t)"),
                                       ALU.mult, ALU.subtract).then_inc(x_lo, 1)

            def evac(i, j, c):
                t = 2 * (i + 1) + j
                dve.wait_ge(z_ready, 2 * t + c + 1)
                if c == 0:
                    wait(dve, t_ready[j], ROUNDS * i + 1)
                    wait(dve, h_ready, t - 2 * ZS + 1)
                v.scalar_tensor_tensor(zring[:, bass.ds(zslot(i + 1, j) + c * HALF, HALF)], z_ps[:, c, :],
                                       sc[:, 7:8], bias_z[:, c * HALF:(c + 1) * HALF], ALU.mult, ALU.add,
                                       accum_out=zsum[:, j, c:c + 1]).then_inc(z_evac, 1)

            def below(i, j):
                p, t = i - 1, 2 * (i - 1) + j
                dve.wait_ge(counted[j], ROUNDS * (p + 1))
                v.scalar_tensor_tensor(w_sb[:, :], zring[:, bass.ds(zslot(p + ZS, j), N)], t_fin[:, j:j + 1],
                                       zring[:, bass.ds(zslot(p + ZS, j), N)], ALU.is_le, ALU.mult).then_inc(masked, 1)
                wait_apart(dve, masked, t + 1)

            def select(i, j):
                p, t = i - 1, 2 * (i - 1) + j
                v.max(out=m8[:, j, :], in_=w_sb[:, :]).then_inc(max8_done, 1)
                dve.wait_ge(max8_done, t + 1)
                v.scalar_tensor_tensor(pick[:, j, :], place[:, :], signs_fin[:, j:j + 1], m8[:, j, :],
                                       ALU.is_equal, ALU.mult, accum_out=thr[:, j:j + 1]).then_inc(picked, 1)
                dve.wait_ge(picked, t + 1)
                v.tensor_scalar(pick[:, j, :], place[:, :], signs_fin[:, j:j + 1], 0.0, ALU.is_equal, ALU.add,
                                accum_out=hit[:, j:j + 1]).then_inc(hit_done, 1)
                dve.wait_ge(hit_done, t + 1)
                if j == 0:
                    wait(dve, flag_ready, p)
                v.scalar_tensor_tensor(ok[:, j:j + 1], m8[:, j, 0:1], t_fin[:, j:j + 1], hit[:, j:j + 1],
                                       ALU.is_lt, ALU.mult).then_inc(selected, 1)

            def general(i):
                p = i - 1
                dve.wait_ge(flag_ready, p + 1)
                v.tensor_copy(flag[:, :], u_ps[0:1, 0:2]).then_inc(flag_read, 1)
                wait_apart(dve, flag_read, p + 1)
                for j in range(2):
                    good = dve.value_load(flag[0:1, j:j + 1], min_val=0, max_val=P)
                    with dve.If(good != P):
                        v.tensor_copy(w_sb[:, :], zring[:, bass.ds(zslot(p + ZS, j), N)])
                        dve.drain()
                        full, last = divmod(TOPK - 1, 8)
                        with dve.Fori(0, full):
                            v.max(out=m8[:, j, :], in_=w_sb[:, :])
                            dve.drain()
                            v.match_replace(out=w_sb[:, :], in_to_replace=m8[:, j, :], in_values=w_sb[:, :],
                                            imm_value=LOWEST)
                            dve.drain()
                        v.max(out=m8[:, j, :], in_=w_sb[:, :])
                        dve.drain()
                        v.tensor_scalar(thr[:, j:j + 1], m8[:, j, last:last + 1], 0.0, None, ALU.max)
                        dve.drain()

            def hidden(i, j):
                p, t = i - 1, 2 * (i - 1) + j
                wait(dve, hT_ready, 4 * t - 4)
                v.scalar_tensor_tensor(h_sb[:, j * N:(j + 1) * N], zring[:, bass.ds(zslot(p + ZS, j), N)],
                                       thr[:, j:j + 1], zring[:, bass.ds(zslot(p + ZS, j), N)],
                                       ALU.is_ge, ALU.mult).then_inc(h_ready, 1)

            def lo_h(i, j, q):
                t = 2 * (i - 2) + j
                dve.wait_ge(h_hi, 4 * t + q + 1)
                wait(dve, m3_done, 4 * t + q - 3)
                v.tensor_tensor(hlo[:, q, :, :].rearrange("p k t -> p (k t)"), tr_ps[q % 2][:, :],
                                hhi[:, q, :, :].rearrange("p k t -> p (k t)"), ALU.subtract).then_inc(h_lo, 1)

            def ln2_in(i, j):
                t = 2 * (i - 2) + j
                dve.wait_ge(m3_done, 4 * t + 4)
                wait(dve, x1_adds, t + 1)
                v.scalar_tensor_tensor(r_sb[:, j, :], o_ps[:, :], sc[:, 11:12],
                                       x1b[:, bass.ds(xslot(i - 2 + XS, j), D)], ALU.mult, ALU.add).then_inc(o_read, 1)
                dve.wait_ge(o_read, t + 1)
                bn(st2, mv2, r_sb[:, j, :], ln2_bn, ln2_stats, t, j)

            def ln3_in(i, j):
                t = 2 * (i - 2) + j
                dve.wait_ge(ln2_stats, t + 1)
                v.scalar_tensor_tensor(r_sb[:, j, :], r_sb[:, j, :], mv2[:, j, 0:1], gamma_bc[:, :],
                                       ALU.subtract, ALU.mult).then_inc(centred, 1)
                dve.wait_ge(centred, t + 1)
                dve.wait_ge(ln2_rstd, t + 1)
                v.scalar_tensor_tensor(r_sb[:, j, :], r_sb[:, j, :], rs2[:, j, 0:1],
                                       x1g[:, bass.ds(xslot(i - 2 + XS, j), D)], ALU.mult, ALU.add).then_inc(v_done, 1)
                dve.wait_ge(v_done, t + 1)
                bn(st3, mv3, r_sb[:, j, :], ln3_bn, ln3_stats, t, j)

            def ln3_out(i, j):
                t = 2 * (i - 2) + j
                dve.wait_ge(ln3_rstd, t + 1)
                wait(dve, stored, 16 * (t - 1))
                v.tensor_scalar(y_sb[:, j, :], r_sb[:, j, :], mv3[:, j, 0:1], rs3[:, j, 0:1],
                                ALU.subtract, ALU.mult).then_inc(y_ready, 1)

            def body(i, A, B, S, Dd):
                if isinstance(i, int) and i == -1:
                    pass
                if S:
                    below(i, 0)
                    select(i, 0)
                if A:
                    ln1_in(i, 0)
                if Dd:
                    lo_h(i, 0, 0)
                if A:
                    ln1_in(i, 1)
                if Dd:
                    lo_h(i, 0, 1)
                if A:
                    ln1_out(i, 0)
                if Dd:
                    lo_h(i, 0, 2)
                if A:
                    ln1_out(i, 1)
                if Dd:
                    lo_h(i, 0, 3)
                if A:
                    lo_x(i, 0)
                if S:
                    below(i, 1)
                if Dd:
                    ln2_in(i, 0)
                if A:
                    evac(i, 0, 0)
                if S:
                    select(i, 1)
                if A:
                    evac(i, 0, 1)
                if Dd:
                    lo_h(i, 1, 0)
                    ln3_in(i, 0)
                    lo_h(i, 1, 1)
                    lo_h(i, 1, 2)
                    ln3_out(i, 0)
                    lo_h(i, 1, 3)
                if A:
                    lo_x(i, 1)
                if S:
                    general(i)
                    hidden(i, 0)
                if A:
                    evac(i, 1, 0)
                if Dd:
                    ln2_in(i, 1)
                if S:
                    hidden(i, 1)
                if Dd:
                    ln3_in(i, 1)
                if A:
                    evac(i, 1, 1)
                if Dd:
                    ln3_out(i, 1)
                if isinstance(i, int) and i == -1:
                    out_weights()

            windows(dve, body)

        @block.tensor
        def _(pe):
            mm = nc.tensor.matmul

            def mm1(i, j):
                t = 2 * (i + 1) + j
                pe.wait_ge(x_loaded, 32 * (i + 2))
                wait(pe, u_read, t)
                if j == 0:
                    wait(pe, flag_read, i - 1)
                for k in range(KD):
                    last = mm(u_ps[:, :], xT_sb[:, k, j * P:(j + 1) * P], weff[:, k, :], start=k == 0, stop=k == KD - 1)
                last.then_inc(u_ready, 1)

            def t1(i, j, Dd):
                t = 2 * (i + 1) + j
                pe.wait_ge(x1_ready, t + 1)
                if Dd:
                    wait(pe, h_lo, 4 * (2 * (i - 2) + j) + 3)
                else:
                    wait(pe, x_lo, t)
                for k in range(KD):
                    last = nc.tensor.transpose(tr_ps[0][:, k * P:(k + 1) * P], x1_sb[:, j, k * P:(k + 1) * P], ident[:, :])
                last.then_inc(x1T_ready, 1)

            def mm2(i, j):
                t = 2 * (i + 1) + j
                pe.wait_ge(x_lo, t + 1)
                for c in range(2):
                    wait(pe, z_evac, 2 * t + c - 1)
                    for k in range(KD):
                        for src in (x1hi, x1lo):
                            for b in range(HALF // BANK):
                                n0 = c * HALF + b * BANK
                                last = mm(z_ps[:, c, b * BANK:(b + 1) * BANK], src[:, j, k, :],
                                          t_syn[:, k, n0:n0 + BANK],
                                          start=k == 0 and src is x1hi, stop=k == KD - 1 and src is x1lo)
                    last.then_inc(z_ready, 1)

            def t2(i, j, q, A):
                t = 2 * (i - 2) + j
                if q == 0:
                    pe.wait_ge(h_ready, t + 1)
                    wait(pe, x_lo, 2 * (i + 1) + j if A else TILES)
                elif q == 1:
                    wait(pe, h_lo, 4 * t)
                else:
                    pe.wait_ge(h_lo, 4 * t + q - 1)
                for b in range(QB):
                    c0 = j * N + (QB * q + b) * P
                    last = nc.tensor.transpose(tr_ps[q % 2][:, b * P:(b + 1) * P], h_sb[:, c0:c0 + P], ident[:, :])
                last.then_inc(hT_ready, 1)

            def mm3(i, j, q):
                t = 2 * (i - 2) + j
                pe.wait_ge(h_lo, 4 * t + q + 1)
                if q == 0:
                    wait(pe, o_read, t)
                for b in range(QB):
                    for src in (hhi, hlo):
                        last = mm(o_ps[:, :], src[:, q, b, :], t_out[:, QB * q + b, :],
                                  start=q == 0 and b == 0 and src is hhi,
                                  stop=q == NQ - 1 and b == QB - 1 and src is hlo)
                last.then_inc(m3_done, 1)

            pe.wait_ge(consts_made, 1)
            pe.wait_ge(part_summed, 1)
            mm(u_ps[:, 0:1], ones[:, :], part[:, 0:1], start=True, stop=True).then_inc(sums_ready, 1)

            def body(i, A, B, S, Dd):
                if isinstance(i, int) and i == -1:
                    pe.wait_ge(weff_made, 1)
                    pe.wait_ge(setup_step, 1)
                if A:
                    mm1(i, 0)
                    mm1(i, 1)
                for j in range(2):
                    if Dd:
                        t2(i, j, 0, A)
                        t2(i, j, 1, A)
                        if isinstance(i, int) and i == 2 and j == 0:
                            pe.wait_ge(t_out_made, 4)
                        mm3(i, j, 0)
                        t2(i, j, 2, A)
                        mm3(i, j, 1)
                        t2(i, j, 3, A)
                        mm3(i, j, 2)
                    if A:
                        t1(i, j, Dd)
                    if Dd:
                        mm3(i, j, 3)
                    if A:
                        if isinstance(i, int) and i == -1 and j == 0:
                            pe.wait_ge(t_syn_made, KD)
                        mm2(i, j)
                    if S and j == 0:
                        wait(pe, selected, 2 * (i - 1) + 2)
                        wait(pe, u_read, 2 * (i + 1) + 2 if A else TILES)
                        mm(u_ps[0:1, 0:2], ones[:, 0:1], ok[:, :], start=True, stop=True).then_inc(flag_ready, 1)
                if isinstance(i, int) and i == -1:
                    pe.wait_ge(part_summed, 2)
                    mm(o_ps[:, 0:1], ones[:, :], part[:, 1:2], start=True, stop=True).then_inc(sums_ready, 1)
                    pe.wait_ge(t_out_made, 4)

            windows(pe, body)


_INS = ["x", "xT", "wT", "dwT", "w_synT", "b_syn", "w_outT", "b_out", "gamma", "beta"]


def kernel(L0_attn_x, L0_attn_W, L0_attn_target_W, L0_attn_delta_W, L0_ffn_W_syn, L0_ffn_b_syn, L0_ffn_W_out,
           L0_ffn_b_out, L0_ffn_gamma, L0_ffn_beta):
    import numpy as np
    import concourse.bacc as bacc
    from concourse.bass_utils import run_bass_kernel_spmd

    x = np.asarray(L0_attn_x)
    shape = x.shape
    x = x.reshape(TOK, D)
    host = {"x": x, "xT": x.T, "wT": np.asarray(L0_attn_W).T, "dwT": np.asarray(L0_attn_delta_W).T,
            "w_synT": np.asarray(L0_ffn_W_syn).T, "b_syn": np.asarray(L0_ffn_b_syn),
            "w_outT": np.asarray(L0_ffn_W_out).T, "b_out": np.asarray(L0_ffn_b_out),
            "gamma": np.asarray(L0_ffn_gamma), "beta": np.asarray(L0_ffn_beta)}
    nc = bacc.Bacc("TRN2", target_bir_lowering=False, num_devices=1)
    arrays, args = {}, []
    for name in _INS:
        a = np.ascontiguousarray(host[name])
        arrays[f"in_{name}"] = a
        args.append(nc.dram_tensor(f"in_{name}", a.shape, mybir.dt.from_np(a.dtype), kind="ExternalInput").ap())
    args.append(nc.dram_tensor("out_y", (TOK, D), FP32, kind="ExternalOutput").ap())
    postln_kernel(nc, *args)
    r = run_bass_kernel_spmd(nc, [arrays], core_ids=[0])
    return r.results[0]["out_y"].reshape(shape)
```
